# Optimizing a Trainium2 kernel written in Bass

```python
import numpy as np
import jax
import jax.numpy as jnp

def _softmax(x, axis=-1):
    return jax.nn.softmax(x, axis=axis)

def _gelu(x):
    return jax.nn.gelu(x, approximate=True)

def _silu(x):
    return jax.nn.silu(x)

def _sigmoid(x):
    return jax.nn.sigmoid(x)

def _layernorm(x, axis=-1, eps=1e-05):
    m = jnp.mean(x, axis=axis, keepdims=True)
    v = jnp.var(x, axis=axis, keepdims=True)
    return (x - m) / jnp.sqrt(v + eps)

def _scatter_add(tgt, idx, src, axis=0):
    return tgt.at[idx].add(src)

def _segment_sum(src, seg, n):
    return jax.ops.segment_sum(src, seg, n)
kernel_name = 'mk_adj_preln_d2_adj_r2_62581c'

def setup_inputs(seed: int=0):
    np.random.seed(seed)
    _w = jnp.asarray

    def _rec_inputs():
        import jax
        import jax.numpy as jnp
        _gk = jax.random.key(seed)
        x = -9.806e-05 + 1 * jax.random.normal(jax.random.fold_in(_gk, 1), (8192, 64), jnp.float32)
        _a = jax.random.bernoulli(jax.random.fold_in(_gk, 2), 0.000488281, (8192, 8192))
        _a = jnp.logical_or(_a, jnp.swapaxes(_a, -1, -2))
        _a = jnp.logical_or(_a, jnp.eye(8192, dtype=bool))
        _af = _a.astype(jnp.float32)
        _af = _af * jax.random.uniform(jax.random.fold_in(_gk, 3), (8192, 8192), jnp.float32, 0.05, 0.0598829)
        adj = _af
        return (x, adj)
    x, adj = _rec_inputs()

    def _L0_gnn_setup():
        import jax, jax.numpy as jnp
        import numpy as np
        N = 4096
        F_IN = 64
        F_OUT = 64
        K = 4
        key = jax.random.key(seed)
        k1, k2, k3 = jax.random.split(key, 3)
        x = jax.random.normal(k1, (N, F_IN), dtype=jnp.float32)
        L = jax.random.normal(k2, (N, N), dtype=jnp.float32) * (1.0 / np.sqrt(N))
        weight = jax.random.normal(k3, (K, F_IN, F_OUT), dtype=jnp.float32) * (1.0 / np.sqrt(F_IN))
        return {'x': x, 'L': L, 'weight': weight}
    _L0_gnn_all = _L0_gnn_setup()
    _L0_gnn_in = {k: v for k, v in _L0_gnn_all.items() if k in ('weight',)}
    del _L0_gnn_all

    def _L1_gnn_setup():
        import jax, jax.numpy as jnp
        import numpy as np
        N, D_IN, D_OUT = (8192, 64, 64)
        AVG_DEG = 32.0
        L2_EPS = 1e-12
        key = jax.random.key(seed)
        kx, ka, kw, kb = jax.random.split(key, 4)
        X = jax.random.normal(kx, (N, D_IN), dtype=jnp.float32)
        adj = (jax.random.uniform(ka, (N, N)) < AVG_DEG / N).astype(jnp.float32)
        bound = 1.0 / np.sqrt(2 * D_IN)
        W = jax.random.uniform(kw, (2 * D_IN, D_OUT), dtype=jnp.float32, minval=-bound, maxval=bound)
        b = jax.random.uniform(kb, (D_OUT,), dtype=jnp.float32, minval=-bound, maxval=bound)
        return {'X': X, 'adj': adj, 'W': W, 'b': b}
    _L1_gnn_all = _L1_gnn_setup()
    _L1_gnn_in = {k: v for k, v in _L1_gnn_all.items() if k in ('W', 'b')}
    del _L1_gnn_all
    return {'x': x, 'adj': adj, 'L0_gnn_weight': _L0_gnn_in['weight'], 'L1_gnn_W': _L1_gnn_in['W'], 'L1_gnn_b': _L1_gnn_in['b']}

def reference(x, adj, L0_gnn_weight, L1_gnn_W, L1_gnn_b):
    import jax
    import jax.numpy as jnp

    def _L0_gnn_ref(x, L, weight):
        import jax, jax.numpy as jnp
        import numpy as np
        N = 4096
        F_IN = 64
        F_OUT = 64
        K = 4
        terms = [x, L @ x]
        for _ in range(2, K):
            terms.append(2.0 * (L @ terms[-1]) - terms[-2])
        feature = jnp.stack(terms, axis=0)
        return jnp.einsum('kni,kio->no', feature, weight)

    def _L1_gnn_ref(X, adj, W, b):
        import jax, jax.numpy as jnp
        import numpy as np
        N, D_IN, D_OUT = (8192, 64, 64)
        AVG_DEG = 32.0
        L2_EPS = 1e-12
        deg = jnp.clip(jnp.sum(adj, axis=1, keepdims=True) + 1.0, 1.0, None)
        h_neigh = (adj @ X + X) / deg
        concat = jnp.concatenate([X, h_neigh], axis=1)
        z = concat @ W + b
        out = jax.nn.relu(z)
        norm = jnp.linalg.norm(out, axis=1, keepdims=True)
        return out / jnp.maximum(norm, L2_EPS)
    h = jnp.maximum(_layernorm(x, axis=-1), 0.0)
    x = x + _L0_gnn_ref(h, adj, L0_gnn_weight)
    h = jnp.maximum(_layernorm(x, axis=-1), 0.0)
    x = x + _L1_gnn_ref(h, adj, L1_gnn_W, L1_gnn_b)
    return x

_drawn_inputs = setup_inputs


def setup_inputs(seed=0):
    import zlib

    import numpy as np

    out = dict(_drawn_inputs(seed))
    spreads = {}
    factors = {'L1_gnn_b': 4.384}
    for name, (base, spread) in spreads.items():
        noise = np.random.default_rng([zlib.crc32(name.encode()), seed]).standard_normal(out[name].shape)
        drawn = base * np.exp(spread * noise) if base else spread * noise
        out[name] = jnp.asarray(drawn.astype(out[name].dtype))
    for name, factor in factors.items():
        out[name] = (out[name] * factor).astype(out[name].dtype)
    return out
```

```python
import concourse.bass as bass
from concourse import mybir
from contextlib import ExitStack

FP32 = mybir.dt.float32
BF16 = mybir.dt.bfloat16
ALU = mybir.AluOpType
ACT = mybir.ActivationFunctionType
AX = mybir.AxisListType

P = 128
N = 8192
F = 64
Q = 4
CH = N // P
CB = 4
NB = CH // CB
BN = CB * P
G = CB * Q
QN = N // Q
W = 4
SW = NB // W
UC = CB * 32
NS = 2
NT = 6
LEAD = 2
SINGLE, PAIR = 0, 1
LN_EPS = 1e-5
L2_EPS = 1e-12


class Row:

    def __init__(self, sweep, C, strips):
        self.sweep, self.C, self.strips = sweep, C, strips
        self.units = [u for _, _, units in strips for u in units]
        self.has_pair = any(kind == PAIR for _, kind in self.units)


def sweep_rows():
    rows = []
    for C in range(NB):
        order = [(C // W + 1 + k) % SW for k in range(SW)]
        strips = []
        for s in order:
            Js = list(range(W * s, W * s + W))
            strips.append((Js[0], W, [(J, SINGLE) for J in Js if J >= C] + [(J, PAIR) for J in Js if J < C]))
        rows.append(Row(1, C, strips))
    for C in reversed(range(NB)):
        strips = []
        for s in reversed(range(C // W, SW)):
            Js = list(range(max(C, W * s), W * s + W))
            units = [(J, PAIR if J > C else SINGLE) for J in reversed(Js)]
            if len(units) > 1 and units[-1][0] == C:
                units[-1], units[-2] = units[-2], units[-1]
            strips.append((Js[0], len(Js), units))
        rows.append(Row(2, C, strips))
    for C in range(NB):
        strips = []
        for s in range(C // W + 1):
            Js = list(range(W * s, min(C, W * s + W - 1) + 1))
            units = [(J, PAIR if J < C else SINGLE) for J in Js]
            if len(units) > 1 and units[-1][0] == C:
                units[-1], units[-2] = units[-2], units[-1]
            strips.append((Js[0], len(Js), units))
        rows.append(Row(3, C, strips))
    for C in range(NB):
        strips = []
        for s in range(C // W, SW):
            Js = list(range(max(C, W * s), W * s + W))
            strips.append((Js[0], len(Js), [(J, SINGLE) for J in Js]))
        rows.append(Row(4, C, strips))
    return rows


def counts_degree(row, J0, w):
    own = row.C // W
    if row.sweep == 1:
        return J0 // W == own or (J0 // W > own and row.C % 2 == 1)
    if row.sweep == 2:
        return J0 // W > own and row.C % 2 == 0
    return row.sweep == 3 and J0 // W < own


def cheb_sage_kernel(nc, x, adj, w_cheb, w_sage, b_sage, out):
    rows = sweep_rows()
    row_index = {(r.sweep, r.C): n for n, r in enumerate(rows)}
    strips = [(n, J0, w, units) for n, r in enumerate(rows) for J0, w, units in r.strips]
    n_units = sum(len(r.units) for r in rows)
    row_start = [sum(len(r.units) for r in rows[:n]) for n in range(len(rows) + 1)]
    strip_start = [sum(len(s[3]) for s in strips[:i]) for i in range(len(strips) + 1)]
    summed_before = [0]
    for n, J0, w, _ in strips:
        summed_before.append(summed_before[-1] + counts_degree(rows[n], J0, w))
    n_summed = summed_before[-1]
    assert n_summed == NB * SW
    x_rows = [n for n, r in enumerate(rows) if r.sweep in (1, 4)]

    def needed_row(row, J, kind):
        if row.sweep == 1:
            return row_index[1, J] if kind == PAIR else None
        if row.sweep == 2:
            return row_index[2, J] if kind == PAIR else row_index[1, J]
        if row.sweep == 3:
            return row_index[3, J] if kind == PAIR else row_index[2, J]
        return row_index[3, J]

    epilogue_at = []
    for n in range(len(rows)):
        if n + 1 == len(rows):
            epilogue_at.append(n_units)
            continue
        J, kind = rows[n + 1].units[0]
        epilogue_at.append(row_start[n + 1] + (needed_row(rows[n + 1], J, kind) != n))

    adj_v = adj.rearrange("(a c r) m -> a r c m", a=Q, r=32)
    x_v = x.rearrange("(a c q) f -> a q c f", a=Q, q=32)
    out_v = out.rearrange("(a c q) f -> a q c f", a=Q, q=32)

    ctx = ExitStack()
    with ctx:
        def sb(name, shape, dt=FP32):
            return ctx.enter_context(nc.sbuf_tensor(name, shape, dt))

        def sem(name):
            return ctx.enter_context(nc.semaphore(name))

        strip_buf = sb("strip_buf", [P, NS, G, W * UC])
        unit_buf = sb("unit_buf", [P, NT, CB, BN])
        vec = sb("vec", [P, CH, 2, F])
        res = sb("res", [P, CH, F])
        part = sb("part", [P, CH, F])
        evac = sb("evac", [P, 2, BN])
        sum_s, sum_p = evac[:, 0, :], evac[:, 1, :]
        vec_t = sb("vec_t", [F + 1, BN])
        junk = sb("junk", [P, 2, W * UC], BF16)
        strip_sums = sb("strip_sums", [P, NB, SW, G])
        row_sums = sb("row_sums", [P, NB, G])
        rdeg = sb("rdeg", [P, CH])
        ident = sb("ident", [P, P])
        fold = sb("fold", [P, Q, P])
        wc = sb("wc", [P, 4, F])
        ws = sb("ws", [P, 2, F])
        rhs_s1 = sb("rhs_s1", [P, 2, F])
        rhs_s2 = sb("rhs_s2", [P, 2, F])
        rhs_w3 = sb("rhs_w3", [P, F])
        rhs_p1 = sb("rhs_p1", [P, F])
        rhs_p2 = sb("rhs_p2", [P, F])
        rhs_p3 = sb("rhs_p3", [P, 2, F])
        rhs_x1 = sb("rhs_x1", [F, F])
        rhs_x4 = sb("rhs_x4", [F + 1, 2, F])
        eps = sb("eps", [P, 1])
        stat = sb("stat", [P, 4, CH])
        tmp = sb("tmp", [P, CB, F])
        tmp2 = sb("tmp2", [P, CB, F])

        ps_single = [ctx.enter_context(nc.psum_tensor(f"ps_single{i}", [P, BN], FP32)) for i in range(2)]
        ps_pair = [ctx.enter_context(nc.psum_tensor(f"ps_pair{i}", [P, BN], FP32)) for i in range(2)]
        ps_lin = ctx.enter_context(nc.psum_tensor("ps_lin", [P, CB, 2, F], FP32))
        ps_tr = ctx.enter_context(nc.psum_tensor("ps_tr", [P, CB, 2, F], FP32))
        ps_xt = ctx.enter_context(nc.psum_tensor("ps_xt", [P, BN], FP32))
        ps_deg = ctx.enter_context(nc.psum_tensor("ps_deg", [P, CH], FP32))

        s_x = sem("x_loaded")
        s_w = sem("weights_loaded")
        s_zero = sem("pool_cleared")
        s_const = sem("constants_ready")
        s_wready = sem("weights_ready")
        s_strip = [sem(f"strip_loaded{i}") for i in range(NS)]
        s_turned = sem("units_turned")
        s_unit = sem("units_done")
        s_junk = sem("groups_summed")
        s_evac = sem("rows_evacuated")
        s_xt = sem("xt_made")
        s_xtc = sem("xt_copied")
        s_lin = sem("rows_combined")
        s_row = sem("rows_stored")
        s_x0 = sem("x_normed")
        s_var = sem("variance_ready")
        s_std = sem("std_ready")
        s_degsum = sem("degree_sums_ready")
        s_deg = sem("degrees_folded")
        s_step = sem("dve_steps")
        s_out = sem("out_stored")

        block = ctx.enter_context(nc.Block())

        @block.sync
        def _(sp):
            for i, (n, J0, w, _) in enumerate(strips):
                row, slot = rows[n], i % NS
                if i >= NS:
                    sp.wait_ge(s_turned, strip_start[i - NS + 1])
                    if summed_before[i - NS + 1] > summed_before[i - NS]:
                        sp.wait_ge(s_junk, G * summed_before[i - NS + 1])
                for ar in range(Q):
                    for a in range(Q):
                        col = a * QN + J0 * UC
                        src = adj_v[ar, :, CB * row.C:CB * row.C + CB, col:col + w * UC]
                        dst = strip_buf[32 * a:32 * a + 32, slot, ar:G:Q, 0:w * UC]
                        sp.dma_start(dst, src).then_inc(s_strip[slot], 16)

        @block.gpsimd
        def _(pool):
            nc.gpsimd.memset(ident[:], 0.0).then_inc(s_zero, 1)
            nc.gpsimd.memset(fold[:], 0.0).then_inc(s_zero, 1)
            nc.gpsimd.memset(rhs_p3[:], 0.0).then_inc(s_zero, 1)
            nc.gpsimd.memset(rhs_x4[:], 0.0).then_inc(s_zero, 1)
            nc.gpsimd.memset(eps[:], LN_EPS).then_inc(s_zero, 1)
            pool.wait_ge(s_zero, 5)
            nc.gpsimd.affine_select(out=ident[:], in_=ident[:], compare_op=ALU.not_equal, fill=1.0, base=0,
                                    pattern=[[-1, P]], channel_multiplier=1).then_inc(s_const, 1)
            for C in range(NB):
                pool.wait_ge(s_row, row_index[4, C] + 1)
                for a in range(Q):
                    pool.dma_start(out_v[a, :, CB * C:CB * C + CB, :],
                                   vec[32 * a:32 * a + 32, CB * C:CB * C + CB, 0, :]).then_inc(s_out, 16)
            pool.wait_ge(s_out, 16 * Q * NB)

        @block.scalar
        def _(act):
            for a in range(Q):
                act.dma_start(res[32 * a:32 * a + 32, :, :], x_v[a]).then_inc(s_x, 16)
            wc_v = w_cheb.rearrange("k i o -> i k o")
            ws_v = w_sage.rearrange("(k i) o -> i k o", k=2)
            for half in (0, F):
                act.dma_start(wc[half:half + F, :, :], wc_v).then_inc(s_w, 16)
                act.dma_start(ws[half:half + F, :, :], ws_v).then_inc(s_w, 16)
            act.wait_ge(s_zero, 5)
            act.dma_start(rhs_x4[F:F + 1, 1, :], b_sage.rearrange("(o f) -> o f", o=1)).then_inc(s_w, 16)
            roots = 0
            for k in range(4):
                act.wait_ge(s_var, k + 1)
                sl = slice(16 * k, 16 * k + 16)
                nc.scalar.activation(stat[:, 2, sl], stat[:, 1, sl], ACT.Sqrt, bias=eps[:], scale=1.0 / F)\
                    .then_inc(s_std, 1)
                roots += 1
            strip = sums = 0
            for n, row in enumerate(rows):
                for J0, w, _ in row.strips:
                    if counts_degree(row, J0, w):
                        slot = strip % NS
                        act.wait_ge(s_strip[slot], 16 * Q * Q * (strip // NS + 1))
                        for g in range(G):
                            if sums >= 2:
                                act.wait_ge(s_junk, sums - 1)
                            nc.scalar.activation(junk[:, sums % 2, 0:w * UC], strip_buf[:, slot, g, 0:w * UC], ACT.Copy,
                                                 accum_out=strip_sums[:, row.C, J0 // W, g:g + 1]).then_inc(s_junk, 1)
                            sums += 1
                    strip += 1
                if n in x_rows:
                    act.wait_ge(s_xt, x_rows.index(n) + 1)
                    if x_rows.index(n):
                        act.wait_ge(s_lin, x_rows[x_rows.index(n) - 1] + 1)
                    nc.scalar.activation(vec_t[0:F, :], ps_xt[0:F, :], ACT.Copy).then_inc(s_xtc, 1)
                act.wait_ge(s_unit, row_start[n + 1])
                if n:
                    act.wait_ge(s_lin, n)
                last = nc.scalar.activation(sum_s, ps_single[n % 2][:], ACT.Copy)
                if row.has_pair:
                    last = nc.scalar.activation(sum_p, ps_pair[n % 2][:], ACT.Copy)
                last.then_inc(s_evac, 1)
                if row.sweep in (3, 4):
                    roots += 1
                    act.wait_ge(s_var, roots)
                    sl = slice(CB * row.C, CB * row.C + CB)
                    if row.sweep == 3:
                        nc.scalar.activation(stat[:, 2, sl], stat[:, 1, sl], ACT.Sqrt, bias=eps[:], scale=1.0 / F)\
                            .then_inc(s_std, 1)
                    else:
                        nc.scalar.activation(stat[:, 2, sl], stat[:, 1, sl], ACT.Sqrt).then_inc(s_std, 1)

        @block.vector
        def _(dve):
            steps = [0]

            def then(ins):
                steps[0] += 1
                ins.then_inc(s_step, 1)
                dve.wait_ge(s_step, steps[0])

            def per_node(ap, k):
                return ap.unsqueeze(2).broadcast_to([P, k, F])

            def layer_norm_relu(dst, src, sl, k, square, root, done):
                then(nc.vector.reduce_sum(stat[:, 0, sl], src, AX.X))
                then(nc.vector.tensor_scalar(stat[:, 0, sl], stat[:, 0, sl], -1.0 / F, None, ALU.mult))
                then(nc.vector.tensor_tensor(dst, src, per_node(stat[:, 0, sl], k), ALU.add))
                then(nc.vector.tensor_tensor(square, dst, dst, ALU.mult))
                nc.vector.reduce_sum(stat[:, 1, sl], square, AX.X).then_inc(s_var, 1)
                dve.wait_ge(s_std, root)
                then(nc.vector.reciprocal(stat[:, 3, sl], stat[:, 2, sl]))
                nc.vector.scalar_tensor_tensor(out=dst, in0=dst, scalar=0.0, in1=per_node(stat[:, 3, sl], k),
                                               op0=ALU.max, op1=ALU.mult).then_inc(done, 1)

            dve.wait_ge(s_x, 16 * Q)
            scratch = evac[:].rearrange("p a n -> p (a n)").rearrange("p (c f) -> p c f", f=F)
            for k in range(4):
                sl = slice(16 * k, 16 * k + 16)
                layer_norm_relu(vec[:, sl, 0, :], res[:, sl, :], sl, 16, scratch, k + 1, s_x0)
            dve.wait_ge(s_w, 16 * 5)
            dve.wait_ge(s_const, 1)
            lo, hi = slice(0, F), slice(F, P)
            nc.vector.memset(vec_t[F:F + 1, :], 1.0)
            nc.vector.tensor_tensor(rhs_s1[:, 0, :], wc[:, 1, :], wc[:, 3, :], ALU.subtract)
            nc.vector.tensor_scalar(rhs_s2[:, 0, :], wc[:, 2, :], 2.0, None, ALU.mult)
            nc.vector.tensor_scalar(rhs_w3[:], wc[:, 3, :], 2.0, None, ALU.mult)
            for dst in (rhs_s1, rhs_s2):
                nc.vector.tensor_tensor(dst[:, 1, :], ident[:, lo], ident[:, hi], ALU.add)
            nc.vector.tensor_tensor(rhs_p1[lo, :], wc[lo, 1, :], wc[lo, 3, :], ALU.subtract)
            nc.vector.tensor_scalar(rhs_p1[hi, :], wc[hi, 2, :], 2.0, None, ALU.mult)
            nc.vector.tensor_scalar(rhs_p2[lo, :], wc[lo, 3, :], 2.0, None, ALU.mult)
            nc.vector.tensor_scalar(rhs_p2[hi, :], wc[hi, 2, :], 2.0, None, ALU.mult)
            nc.vector.tensor_scalar(rhs_p3[lo, 0, :], wc[lo, 3, :], 2.0, None, ALU.mult)
            nc.vector.tensor_copy(rhs_p3[hi, 1, :], ws[hi, 1, :])
            nc.vector.tensor_tensor(rhs_x1[:], wc[lo, 0, :], wc[lo, 2, :], ALU.subtract)
            nc.vector.tensor_copy(rhs_x4[lo, 0, :], ws[lo, 1, :])
            nc.vector.tensor_copy(rhs_x4[lo, 1, :], ws[lo, 0, :])
            for a in range(Q):
                for b in range(Q):
                    last = nc.vector.tensor_copy(fold[32 * b:32 * b + 32, a, 32 * a:32 * a + 32],
                                                 ident[32 * b:32 * b + 32, 32 * b:32 * b + 32])
            last.then_inc(s_wready, 1)

            roots = [4]

            def epilogue(n):
                row = rows[n]
                C = row.C
                sl = slice(CB * C, CB * C + CB)
                x1, pt = res[:, sl, :], part[:, sl, :]
                lin, new, tr = ps_lin[:, :, 0, :], ps_lin[:, :, 1, :], ps_tr
                if row.sweep == 4 and C == 0:
                    dve.wait_ge(s_junk, G * n_summed)
                    nc.vector.reduce_sum(row_sums[:], strip_sums[:].rearrange("p c s g -> p c g s"), AX.X)\
                        .then_inc(s_degsum, 1)
                    dve.wait_ge(s_deg, 1)
                    then(nc.vector.tensor_scalar(rdeg[:], ps_deg[:], 1.0, 1.0, ALU.add, ALU.max))
                    then(nc.vector.reciprocal(rdeg[:], rdeg[:]))
                dve.wait_ge(s_lin, n + 1)
                if row.sweep == 1:
                    nc.vector.tensor_tensor(x1, x1, lin, ALU.add)
                    if row.has_pair:
                        nc.vector.tensor_copy(pt, tr[:, :, 1, :])
                        then(nc.vector.tensor_copy(vec[:, sl, 1, :], new))
                        last = nc.vector.tensor_tensor(vec[:, sl, 1, :], vec[:, sl, 1, :], tr[:, :, 0, :], ALU.add)
                    else:
                        nc.vector.memset(pt, 0.0)
                        last = nc.vector.tensor_copy(vec[:, sl, 1, :], new)
                elif row.sweep == 2:
                    then(nc.vector.tensor_tensor(tmp[:], pt, new, ALU.add))
                    nc.vector.tensor_tensor(x1, x1, lin, ALU.add)
                    if row.has_pair:
                        then(nc.vector.tensor_tensor(tmp[:], tmp[:], tr[:, :, 1, :], ALU.add))
                    last = nc.vector.scalar_tensor_tensor(out=vec[:, sl, 0, :], in0=tmp[:], scalar=2.0, in1=vec[:, sl, 0, :],
                                                          op0=ALU.mult, op1=ALU.subtract)
                elif row.sweep == 3:
                    then(nc.vector.tensor_tensor(x1, x1, lin, ALU.add))
                    if row.has_pair:
                        nc.vector.tensor_copy(pt, new)
                    else:
                        nc.vector.memset(pt, 0.0)
                    roots[0] += 1
                    layer_norm_relu(vec[:, sl, 1, :], x1, sl, CB, tmp[:], roots[0], s_row)
                    return
                else:
                    then(nc.vector.tensor_tensor(tmp[:], pt, lin, ALU.add))
                    then(nc.vector.tensor_tensor(tmp[:], tmp[:], per_node(rdeg[:, sl], CB), ALU.mult))
                    then(nc.vector.tensor_tensor(tmp[:], tmp[:], new, ALU.add))
                    then(nc.vector.tensor_scalar(tmp[:], tmp[:], 0.0, None, ALU.max))
                    then(nc.vector.tensor_tensor(tmp2[:], tmp[:], tmp[:], ALU.mult))
                    nc.vector.reduce_sum(stat[:, 1, sl], tmp2[:], AX.X).then_inc(s_var, 1)
                    roots[0] += 1
                    dve.wait_ge(s_std, roots[0])
                    then(nc.vector.tensor_scalar(stat[:, 3, sl], stat[:, 2, sl], L2_EPS, None, ALU.max))
                    then(nc.vector.reciprocal(stat[:, 3, sl], stat[:, 3, sl]))
                    then(nc.vector.tensor_tensor(tmp[:], tmp[:], per_node(stat[:, 3, sl], CB), ALU.mult))
                    last = nc.vector.tensor_tensor(vec[:, sl, 0, :], tmp[:], x1, ALU.add)
                if row.sweep == 2:
                    if row.has_pair:
                        then(last)
                        last = nc.vector.tensor_copy(pt, tr[:, :, 0, :])
                    else:
                        then(last)
                        last = nc.vector.memset(pt, 0.0)
                last.then_inc(s_row, 1)

            pending = 0
            u = 0
            for i, (n, J0, w, units) in enumerate(strips):
                slot = i % NS
                dve.wait_ge(s_strip[slot], 16 * Q * Q * (i // NS + 1))
                for J, _ in units:
                    if u >= NT:
                        dve.wait_ge(s_unit, u - NT + 1)
                    col = (J - J0) * UC
                    src = strip_buf[:, slot, :, col:col + UC].rearrange("p g (c q) -> p g c q", q=32)
                    dst = unit_buf[:, u % NT, :, :].rearrange("p c (g r) -> p g c r", r=32)
                    nc.vector.transpose(dst, src).then_inc(s_turned, 1)
                    u += 1
                    if pending < len(rows) and u >= min(epilogue_at[pending] + LEAD, n_units):
                        epilogue(pending)
                        pending += 1
            while pending < len(rows):
                epilogue(pending)
                pending += 1

        @block.tensor
        def _(pe):
            pe.wait_ge(s_wready, 1)
            stored = [0]
            xts = [0]

            def need_rows(k):
                if k > stored[0]:
                    pe.wait_ge(s_row, k)
                    stored[0] = k

            def transpose_vector(n):
                row = rows[n]
                if row.sweep == 4:
                    need_rows(row_index[3, row.C] + 1)
                if xts[0]:
                    pe.wait_ge(s_xtc, xts[0])
                src_slot = 0 if row.sweep == 1 else 1
                for c in range(CB):
                    last = nc.tensor.transpose(ps_xt[0:F, P * c:P * c + P], vec[:, CB * row.C + c, src_slot, :], ident[:])
                last.then_inc(s_xt, 1)
                xts[0] += 1

            def epilogue(n):
                row = rows[n]
                pe.wait_ge(s_evac, n + 1)
                need_rows(n)
                if n in x_rows:
                    pe.wait_ge(s_xtc, x_rows.index(n) + 1)
                if row.sweep == 4 and row.C == 0:
                    pe.wait_ge(s_degsum, 1)
                    for a in range(Q):
                        last = nc.tensor.matmul(ps_deg[:], fold[:, a, :],
                                                row_sums[:].rearrange("p c (k a) -> p (c k) a", a=Q)[:, :, a],
                                                start=(a == 0), stop=(a == Q - 1))
                    last.then_inc(s_deg, 1)
                for c in range(CB):
                    cols = slice(P * c, P * c + P)
                    S, PR, XT = sum_s[:, cols], sum_p[:, cols], vec_t[:, cols]
                    lin, both = ps_lin[:, c, 0, :], ps_lin[:, c, :, :]
                    if row.sweep == 1:
                        nc.tensor.matmul(both, S, rhs_s1[:], start=True, stop=False)
                        if row.has_pair:
                            nc.tensor.matmul(lin, PR, rhs_p1[:], start=False, stop=False)
                        last = nc.tensor.matmul(lin, XT[0:F, :], rhs_x1[:], start=False, stop=True)
                    elif row.sweep == 2:
                        last = nc.tensor.matmul(both, S, rhs_s2[:], start=True, stop=not row.has_pair)
                        if row.has_pair:
                            last = nc.tensor.matmul(lin, PR, rhs_p2[:], start=False, stop=True)
                    elif row.sweep == 3:
                        if row.has_pair:
                            nc.tensor.matmul(both, PR, rhs_p3[:], start=True, stop=False)
                        last = nc.tensor.matmul(lin, S, rhs_w3[:], start=not row.has_pair, stop=True)
                    else:
                        nc.tensor.matmul(both, XT, rhs_x4[:], start=True, stop=False)
                        last = nc.tensor.matmul(lin, S, ws[:, 1, :], start=False, stop=True)
                if row.sweep in (1, 2) and row.has_pair:
                    for c in range(CB):
                        last = nc.tensor.transpose(ps_tr[:, c, :, :], sum_p[:, P * c:P * c + P], ident[:])
                last.then_inc(s_lin, 1)

            u = 0
            pending = 0
            for n, row in enumerate(rows):
                pair_at = [k for k, (_, kind) in enumerate(row.units) if kind == PAIR]
                single_at = [k for k, (_, kind) in enumerate(row.units) if kind == SINGLE]
                single_slot = {1: 0, 2: 1, 3: 0, 4: 1}[row.sweep]
                if row.sweep == 1 and n == 0:
                    pe.wait_ge(s_x0, 4)
                for k, (J, kind) in enumerate(row.units):
                    if pending < n and u == epilogue_at[pending]:
                        epilogue(pending)
                        pending += 1
                    if k == len(row.units) - 1 and n in x_rows:
                        transpose_vector(n)
                    if k == 0 and n >= 2:
                        pe.wait_ge(s_evac, n - 1)
                    need = needed_row(row, J, kind)
                    if need is not None:
                        need_rows(need + 1)
                    pe.wait_ge(s_turned, u + 1)
                    for c in range(CB):
                        moving = unit_buf[:, u % NT, c, :]
                        if kind == PAIR:
                            last = nc.tensor.matmul(ps_pair[n % 2][:], vec[:, CB * J + c, :, :], moving,
                                                    start=(k == pair_at[0] and c == 0),
                                                    stop=(k == pair_at[-1] and c == CB - 1))
                        else:
                            half = F * (c % 2)
                            last = nc.tensor.matmul(ps_single[n % 2][half:half + F, :],
                                                    vec[:, CB * J + c, single_slot, :], moving,
                                                    start=(k == single_at[0] and c < 2),
                                                    stop=(k == single_at[-1] and c >= CB - 2))
                    last.then_inc(s_unit, 1)
                    u += 1
            while pending < len(rows):
                epilogue(pending)
                pending += 1


_INS = ['x', 'adj', 'L0_gnn_weight', 'L1_gnn_W', 'L1_gnn_b']
_OUTS = [((N, F), 'float32')]


def kernel(**inputs):
    import numpy as _np
    import concourse.bacc as _bacc
    from concourse import mybir as _mybir
    from concourse.bass_utils import run_bass_kernel_spmd as _run

    nc = _bacc.Bacc("TRN2", target_bir_lowering=False, num_devices=1)
    arrays, args = {}, []
    for name in _INS:
        a = _np.ascontiguousarray(inputs[name])
        arrays[f"in_{name}_dram"] = a
        args.append(nc.dram_tensor(f"in_{name}_dram", a.shape, _mybir.dt.from_np(a.dtype), kind="ExternalInput").ap())
    for i, (shape, dtype) in enumerate(_OUTS):
        args.append(nc.dram_tensor(f"out_{i}_dram", shape, _mybir.dt.from_np(_np.dtype(dtype)), kind="ExternalOutput").ap())
    cheb_sage_kernel(nc, *args)
    r = _run(nc, [arrays], core_ids=[0])
    return r.results[0]["out_0_dram"]
```

```python
import concourse.bass as bass
from concourse import mybir
from contextlib import ExitStack

FP32 = mybir.dt.float32
ALU = mybir.AluOpType
ACT = mybir.ActivationFunctionType
AX = mybir.AxisListType

P = 128
N = 8192
F = 64
Q = 4
CH = N // P
CB = 4
NB = CH // CB
BN = CB * P
G = CB * Q
QN = N // Q
W = 4
SW = NB // W
UC = CB * 32
RING = 16
NSEM = 6
LEAD = 5
SINGLE, PAIR = 0, 1
LN_EPS = 1e-5
L2_EPS = 1e-12


class Row:

    def __init__(self, sweep, C, strips):
        self.sweep, self.C, self.strips = sweep, C, strips
        self.units = [u for _, _, units in strips for u in units]
        self.has_pair = any(kind == PAIR for _, kind in self.units)


def sweep_rows():
    rows = []
    for C in range(NB):
        order = [(C // W + 1 + k) % SW for k in range(SW)]
        strips = []
        for s in order:
            Js = list(range(W * s, W * s + W))
            strips.append((Js[0], W, [(J, SINGLE) for J in Js if J >= C] + [(J, PAIR) for J in Js if J < C]))
        rows.append(Row(1, C, strips))
    for C in reversed(range(NB)):
        strips = []
        for s in reversed(range(C // W, SW)):
            Js = list(range(max(C, W * s), W * s + W))
            units = [(J, PAIR if J > C else SINGLE) for J in reversed(Js)]
            if len(units) > 1 and units[-1][0] == C:
                units[-1], units[-2] = units[-2], units[-1]
            strips.append((Js[0], len(Js), units))
        rows.append(Row(2, C, strips))
    for C in range(NB):
        strips = []
        for s in range(C // W + 1):
            Js = list(range(W * s, min(C, W * s + W - 1) + 1))
            units = [(J, PAIR if J < C else SINGLE) for J in Js]
            if len(units) > 1 and units[-1][0] == C:
                units[-1], units[-2] = units[-2], units[-1]
            strips.append((Js[0], len(Js), units))
        rows.append(Row(3, C, strips))
    for C in range(NB):
        strips = []
        for s in range(C // W, SW):
            Js = list(range(max(C, W * s), W * s + W))
            strips.append((Js[0], len(Js), [(J, SINGLE) for J in Js]))
        rows.append(Row(4, C, strips))
    return rows


def ring_places(strips):
    at, places, live = 0, [], []
    for i, (_, _, w, _) in enumerate(strips):
        if at + w > RING:
            at = 0
        clash = [k for k, lo, hi in live if lo < at + w and hi > at]
        before = max(clash, default=-1) + 1
        before = max(before, i - NSEM + 1)
        live = [(k, lo, hi) for k, lo, hi in live if k >= before] + [(i, at, at + w)]
        places.append((at, before))
        at += w
    return places


def cheb_sage_kernel(nc, x, adj, w_cheb, w_sage, b_sage, out):
    rows = sweep_rows()
    row_index = {(r.sweep, r.C): n for n, r in enumerate(rows)}
    strips = [(n, J0, w, units) for n, r in enumerate(rows) for J0, w, units in r.strips]
    n_units = sum(len(r.units) for r in rows)
    row_start = [sum(len(r.units) for r in rows[:n]) for n in range(len(rows) + 1)]
    strip_start = [sum(len(s[3]) for s in strips[:i]) for i in range(len(strips) + 1)]
    first_strip = [sum(len(r.strips) for r in rows[:n]) for n in range(len(rows) + 1)]
    places = ring_places(strips)
    x_rows = [n for n, r in enumerate(rows) if r.sweep in (1, 4)]

    def needed_row(row, J, kind):
        if row.sweep == 1:
            return row_index[1, J] if kind == PAIR else None
        if row.sweep == 2:
            return row_index[2, J] if kind == PAIR else row_index[1, J]
        if row.sweep == 3:
            return row_index[3, J] if kind == PAIR else row_index[2, J]
        return row_index[3, J]

    epilogue_at = []
    for n in range(len(rows)):
        if n + 1 == len(rows):
            epilogue_at.append(n_units)
            continue
        J, kind = rows[n + 1].units[0]
        epilogue_at.append(row_start[n + 1] + (needed_row(rows[n + 1], J, kind) != n))

    begin_at = [min(epilogue_at[n] + LEAD, row_start[min(n + 2, len(rows))]) for n in range(len(rows))]

    adj_v = adj.rearrange("(a c r) m -> a r c m", a=Q, r=32)
    x_v = x.rearrange("(a c q) f -> a q c f", a=Q, q=32)
    out_v = out.rearrange("(a c q) f -> a q c f", a=Q, q=32)

    ctx = ExitStack()
    with ctx:
        def sb(name, shape, dt=FP32):
            return ctx.enter_context(nc.sbuf_tensor(name, shape, dt))

        def sem(name):
            return ctx.enter_context(nc.semaphore(name))

        ring = sb("ring", [P, RING * G * UC])
        vec = sb("vec", [P, CH, 2, F])
        res = sb("res", [P, CH, F])
        part = sb("part", [P, CH, F])
        evac = sb("evac", [P, 2, BN])
        sum_s, sum_p = evac[:, 0, :], evac[:, 1, :]
        vec_t = sb("vec_t", [F + 1, BN])
        strip_sums = sb("strip_sums", [P, 2, SW, G])
        row_sums = sb("row_sums", [P, NB, G])
        rdeg = sb("rdeg", [P, CH])
        ident = sb("ident", [P, P])
        fold = sb("fold", [P, 32])
        ws = sb("ws", [P, 2, F])
        rhs_s1 = sb("rhs_s1", [P, 2, F])
        rhs_s2 = sb("rhs_s2", [P, 2, F])
        rhs_w3 = sb("rhs_w3", [P, F])
        rhs_p1 = sb("rhs_p1", [P, F])
        rhs_p2 = sb("rhs_p2", [P, F])
        rhs_p3 = sb("rhs_p3", [P, 2, F])
        rhs_x1 = sb("rhs_x1", [F, F])
        rhs_x4 = sb("rhs_x4", [F + 1, 2, F])
        eps = sb("eps", [P, 1])
        stat = sb("stat", [P, 4, CH])
        tmp = sb("tmp", [P, CB, F])
        wc = tmp

        ps_single = [ctx.enter_context(nc.psum_tensor(f"ps_single{i}", [P, BN], FP32)) for i in range(2)]
        ps_pair = [ctx.enter_context(nc.psum_tensor(f"ps_pair{i}", [P, BN], FP32)) for i in range(2)]
        ps_lin = ctx.enter_context(nc.psum_tensor("ps_lin", [P, CB, 2, F], FP32))
        ps_tr = ctx.enter_context(nc.psum_tensor("ps_tr", [P, CB, 2, F], FP32))
        ps_xt = ctx.enter_context(nc.psum_tensor("ps_xt", [P, BN], FP32))
        ps_deg = ctx.enter_context(nc.psum_tensor("ps_deg", [P, CH], FP32))

        def strip_of(i):
            w = strips[i][2]
            at = places[i][0] * G * UC
            return ring[:, at:at + G * w * UC].rearrange("p (g m) -> p g m", g=G)

        s_x = [sem(f"x_loaded{h}") for h in range(2)]
        s_cent = sem("x_centred")
        s_sq = sem("x_squared")
        s_w = sem("weights_loaded")
        s_zero = sem("pool_cleared")
        s_const = sem("constants_ready")
        s_wready = sem("weights_ready")
        s_strip = [sem(f"strip_loaded{i}") for i in range(NSEM)]
        s_turned = sem("units_turned")
        s_unit = sem("units_done")
        s_summed = sem("strips_summed")
        s_evac = sem("rows_evacuated")
        s_xt = sem("xt_made")
        s_xtc = sem("xt_copied")
        s_lin = sem("rows_combined")
        s_row = sem("rows_stored")
        s_x0 = sem("x_normed")
        s_var = sem("variance_ready")
        s_std = sem("std_ready")
        s_degsum = sem("degree_sums_ready")
        s_deg = sem("degrees_folded")
        s_step = sem("dve_steps")
        s_out = sem("out_stored")

        block = ctx.enter_context(nc.Block())

        @block.sync
        def _(sp):
            for h in range(2):
                for a in range(Q):
                    sp.dma_start(res[32 * a:32 * a + 32, 32 * h:32 * h + 32, :], x_v[a, :, 32 * h:32 * h + 32, :])\
                        .then_inc(s_x[h], 16)
            for i, (n, J0, w, _) in enumerate(strips):
                row = rows[n]
                if places[i][1] > 0:
                    sp.wait_ge(s_unit, strip_start[places[i][1]])
                for ar in range(Q):
                    for a in range(Q):
                        col = a * QN + J0 * UC
                        src = adj_v[ar, :, CB * row.C:CB * row.C + CB, col:col + w * UC]
                        dst = strip_of(i)[32 * a:32 * a + 32, ar:G:Q, :]
                        sp.dma_start(dst, src).then_inc(s_strip[i % NSEM], 16)

        @block.gpsimd
        def _(pool):
            nc.gpsimd.memset(ident[:], 0.0).then_inc(s_zero, 1)
            nc.gpsimd.memset(rhs_p3[:], 0.0).then_inc(s_zero, 1)
            nc.gpsimd.memset(rhs_x4[:], 0.0).then_inc(s_zero, 1)
            nc.gpsimd.memset(eps[:], LN_EPS).then_inc(s_zero, 1)
            pool.wait_ge(s_zero, 4)
            nc.gpsimd.affine_select(out=ident[:], in_=ident[:], compare_op=ALU.not_equal, fill=1.0, base=0,
                                    pattern=[[-1, P]], channel_multiplier=1).then_inc(s_const, 1)
            for C in range(NB):
                pool.wait_ge(s_row, row_index[4, C] + 1)
                for a in range(Q):
                    pool.dma_start(out_v[a, :, CB * C:CB * C + CB, :],
                                   vec[32 * a:32 * a + 32, CB * C:CB * C + CB, 0, :]).then_inc(s_out, 16)
            pool.wait_ge(s_out, 16 * Q * NB)

        @block.scalar
        def _(act):
            wc_v = w_cheb.rearrange("k i o -> i k o")
            ws_v = w_sage.rearrange("(k i) o -> i k o", k=2)
            for half in (0, F):
                act.dma_start(wc[half:half + F, :, :], wc_v).then_inc(s_w, 16)
                act.dma_start(ws[half:half + F, :, :], ws_v).then_inc(s_w, 16)
            act.wait_ge(s_zero, 4)
            act.dma_start(rhs_x4[F:F + 1, 1, :], b_sage.rearrange("(o f) -> o f", o=1)).then_inc(s_w, 16)
            quarter = [slice(16 * k, 16 * k + 16) for k in range(4)]

            def root_of_variance(number, sl):
                act.wait_ge(s_var, number)
                nc.scalar.activation(stat[:, 2, sl], stat[:, 1, sl], ACT.Sqrt, bias=eps[:], scale=1.0 / F)\
                    .then_inc(s_std, 1)

            for k in range(4):
                act.wait_ge(s_cent, k + 1)
                nc.scalar.activation(part[:, quarter[k], :], vec[:, quarter[k], 0, :], ACT.Square).then_inc(s_sq, 1)
                if k:
                    root_of_variance(k, quarter[k - 1])
            root_of_variance(4, quarter[3])
            roots = 4
            def sum_rows(i):
                n, J0, w, _ = strips[i]
                C = rows[n].C
                if rows[n].sweep > 1:
                    return
                act.wait_ge(s_strip[i % NSEM], 16 * Q * Q * (i // NSEM + 1))
                if C >= 2:
                    act.wait_ge(s_degsum, C - 1)
                for g in range(G):
                    last = nc.scalar.activation(strip_of(i)[:, g, :], strip_of(i)[:, g, :], ACT.Copy,
                                                accum_out=strip_sums[:, C % 2, J0 // W, g:g + 1])
                last.then_inc(s_summed, 1)

            sum_rows(0)
            for n, row in enumerate(rows):
                first = first_strip[n]
                for i in range(first + 1, first + 2):
                    if i < first_strip[n + 1]:
                        sum_rows(i)
                if n in x_rows:
                    act.wait_ge(s_xt, x_rows.index(n) + 1)
                    if x_rows.index(n):
                        act.wait_ge(s_lin, x_rows[x_rows.index(n) - 1] + 1)
                    nc.scalar.activation(vec_t[0:F, :], ps_xt[0:F, :], ACT.Copy).then_inc(s_xtc, 1)
                for i in range(first + 2, first_strip[n + 1]):
                    sum_rows(i)
                if n + 1 < len(rows):
                    sum_rows(first_strip[n + 1])
                act.wait_ge(s_unit, row_start[n + 1])
                if n:
                    act.wait_ge(s_lin, n)
                last = nc.scalar.activation(sum_s, ps_single[n % 2][:], ACT.Copy)
                if row.has_pair:
                    last = nc.scalar.activation(sum_p, ps_pair[n % 2][:], ACT.Copy)
                last.then_inc(s_evac, 1)
                if row.sweep in (3, 4):
                    roots += 1
                    sl = slice(CB * row.C, CB * row.C + CB)
                    if row.sweep == 3:
                        root_of_variance(roots, sl)
                    else:
                        act.wait_ge(s_var, roots)
                        nc.scalar.activation(stat[:, 2, sl], stat[:, 1, sl], ACT.Sqrt).then_inc(s_std, 1)

        @block.vector
        def _(dve):
            steps = [0]

            def then(ins):
                steps[0] += 1
                ins.then_inc(s_step, 1)
                dve.wait_ge(s_step, steps[0])

            def per_node(ap, k):
                return ap.unsqueeze(2).broadcast_to([P, k, F])

            def centre(dst, src, sl, k):
                then(nc.vector.reduce_sum(stat[:, 0, sl], src, AX.X))
                then(nc.vector.tensor_scalar(stat[:, 0, sl], stat[:, 0, sl], -1.0 / F, None, ALU.mult))
                return nc.vector.tensor_tensor(dst, src, per_node(stat[:, 0, sl], k), ALU.add)

            def scale_relu(dst, sl, k, root):
                dve.wait_ge(s_std, root)
                then(nc.vector.reciprocal(stat[:, 3, sl], stat[:, 2, sl]))
                return nc.vector.scalar_tensor_tensor(out=dst, in0=dst, scalar=0.0, in1=per_node(stat[:, 3, sl], k),
                                                      op0=ALU.max, op1=ALU.mult)

            quarter = [slice(16 * k, 16 * k + 16) for k in range(4)]
            for k in range(6):
                if k < 4:
                    dve.wait_ge(s_x[k // 2], 16 * Q)
                    centre(vec[:, quarter[k], 0, :], res[:, quarter[k], :], quarter[k], 16).then_inc(s_cent, 1)
                if 1 <= k < 5:
                    dve.wait_ge(s_sq, k)
                    nc.vector.reduce_sum(stat[:, 1, quarter[k - 1]], part[:, quarter[k - 1], :], AX.X).then_inc(s_var, 1)
                if k >= 2:
                    scale_relu(vec[:, quarter[k - 2], 0, :], quarter[k - 2], 16, k - 1).then_inc(s_x0, 1)
            dve.wait_ge(s_w, 16 * 5)
            dve.wait_ge(s_const, 1)
            lo, hi = slice(0, F), slice(F, P)
            nc.vector.memset(vec_t[F:F + 1, :], 1.0)
            nc.vector.tensor_tensor(rhs_s1[:, 0, :], wc[:, 1, :], wc[:, 3, :], ALU.subtract)
            nc.vector.tensor_scalar(rhs_s2[:, 0, :], wc[:, 2, :], 2.0, None, ALU.mult)
            nc.vector.tensor_scalar(rhs_w3[:], wc[:, 3, :], 2.0, None, ALU.mult)
            for dst in (rhs_s1, rhs_s2):
                nc.vector.tensor_tensor(dst[:, 1, :], ident[:, lo], ident[:, hi], ALU.add)
            nc.vector.tensor_tensor(rhs_p1[lo, :], wc[lo, 1, :], wc[lo, 3, :], ALU.subtract)
            nc.vector.tensor_scalar(rhs_p1[hi, :], wc[hi, 2, :], 2.0, None, ALU.mult)
            nc.vector.tensor_scalar(rhs_p2[lo, :], wc[lo, 3, :], 2.0, None, ALU.mult)
            nc.vector.tensor_scalar(rhs_p2[hi, :], wc[hi, 2, :], 2.0, None, ALU.mult)
            nc.vector.tensor_scalar(rhs_p3[lo, 0, :], wc[lo, 3, :], 2.0, None, ALU.mult)
            nc.vector.tensor_copy(rhs_p3[hi, 1, :], ws[hi, 1, :])
            nc.vector.tensor_tensor(rhs_x1[:], wc[lo, 0, :], wc[lo, 2, :], ALU.subtract)
            nc.vector.tensor_copy(rhs_x4[lo, 0, :], ws[lo, 1, :])
            nc.vector.tensor_copy(rhs_x4[lo, 1, :], ws[lo, 0, :])
            for a in range(Q):
                last = nc.vector.tensor_copy(fold[32 * a:32 * a + 32, :], ident[32 * a:32 * a + 32, 32 * a:32 * a + 32])
            last.then_inc(s_wready, 1)

            roots = [4]

            def epilogue(n):
                row = rows[n]
                C = row.C
                sl = slice(CB * C, CB * C + CB)
                x1, pt = res[:, sl, :], part[:, sl, :]
                lin, new, tr = ps_lin[:, :, 0, :], ps_lin[:, :, 1, :], ps_tr
                if row.sweep == 4 and C == 0:
                    dve.wait_ge(s_deg, 1)
                    then(nc.vector.tensor_scalar(rdeg[:], ps_deg[:], 1.0, 1.0, ALU.add, ALU.max))
                    then(nc.vector.reciprocal(rdeg[:], rdeg[:]))
                dve.wait_ge(s_lin, n + 1)
                if row.sweep == 1:
                    dve.wait_ge(s_summed, SW * (C + 1))
                    nc.vector.reduce_sum(row_sums[:, C, :], strip_sums[:, C % 2].rearrange("p s g -> p g s"), AX.X)\
                        .then_inc(s_degsum, 1)
                    nc.vector.tensor_tensor(x1, x1, lin, ALU.add)
                    if row.has_pair:
                        nc.vector.tensor_copy(pt, tr[:, :, 1, :])
                        then(nc.vector.tensor_copy(vec[:, sl, 1, :], new))
                        last = nc.vector.tensor_tensor(vec[:, sl, 1, :], vec[:, sl, 1, :], tr[:, :, 0, :], ALU.add)
                    else:
                        nc.vector.memset(pt, 0.0)
                        last = nc.vector.tensor_copy(vec[:, sl, 1, :], new)
                elif row.sweep == 2:
                    then(nc.vector.tensor_tensor(tmp[:], pt, new, ALU.add))
                    nc.vector.tensor_tensor(x1, x1, lin, ALU.add)
                    if row.has_pair:
                        then(nc.vector.tensor_tensor(tmp[:], tmp[:], tr[:, :, 1, :], ALU.add))
                    if row.has_pair:
                        nc.vector.tensor_copy(pt, tr[:, :, 0, :])
                    else:
                        nc.vector.memset(pt, 0.0)
                    last = nc.vector.scalar_tensor_tensor(out=vec[:, sl, 0, :], in0=tmp[:], scalar=2.0,
                                                          in1=vec[:, sl, 0, :], op0=ALU.mult, op1=ALU.subtract)
                elif row.sweep == 3:
                    then(nc.vector.tensor_tensor(x1, x1, lin, ALU.add))
                    if row.has_pair:
                        nc.vector.tensor_copy(pt, new)
                    else:
                        nc.vector.memset(pt, 0.0)
                    then(centre(vec[:, sl, 1, :], x1, sl, CB))
                    then(nc.vector.tensor_tensor(tmp[:], vec[:, sl, 1, :], vec[:, sl, 1, :], ALU.mult))
                    nc.vector.reduce_sum(stat[:, 1, sl], tmp[:], AX.X).then_inc(s_var, 1)
                    return
                else:
                    then(nc.vector.tensor_tensor(tmp[:], pt, lin, ALU.add))
                    then(nc.vector.tensor_tensor(tmp[:], tmp[:], per_node(rdeg[:, sl], CB), ALU.mult))
                    then(nc.vector.tensor_tensor(tmp[:], tmp[:], new, ALU.add))
                    then(nc.vector.tensor_scalar(tmp[:], tmp[:], 0.0, None, ALU.max))
                    then(nc.vector.tensor_tensor(vec[:, sl, 0, :], tmp[:], tmp[:], ALU.mult))
                    nc.vector.reduce_sum(stat[:, 1, sl], vec[:, sl, 0, :], AX.X).then_inc(s_var, 1)
                    return
                last.then_inc(s_row, 1)

            def epilogue_end(n):
                row = rows[n]
                sl = slice(CB * row.C, CB * row.C + CB)
                roots[0] += 1
                if row.sweep == 3:
                    last = scale_relu(vec[:, sl, 1, :], sl, CB, roots[0])
                else:
                    dve.wait_ge(s_std, roots[0])
                    then(nc.vector.tensor_scalar(stat[:, 3, sl], stat[:, 2, sl], L2_EPS, None, ALU.max))
                    then(nc.vector.reciprocal(stat[:, 3, sl], stat[:, 3, sl]))
                    then(nc.vector.tensor_tensor(tmp[:], tmp[:], per_node(stat[:, 3, sl], CB), ALU.mult))
                    last = nc.vector.tensor_tensor(vec[:, sl, 0, :], tmp[:], res[:, sl, :], ALU.add)
                last.then_inc(s_row, 1)

            begun = ended = 0
            u = 0
            for i, (n, J0, w, units) in enumerate(strips):
                dve.wait_ge(s_strip[i % NSEM], 16 * Q * Q * (i // NSEM + 1))
                if rows[n].sweep == 1:
                    dve.wait_ge(s_summed, i + 1)
                for J, _ in units:
                    col = (J - J0) * UC
                    blocks = strip_of(i)[:, :, col:col + UC].rearrange("p g (c q) -> p g c q", q=32)
                    nc.vector.transpose(blocks, blocks).then_inc(s_turned, 1)
                    u += 1
                    if ended < begun and u >= min(begin_at[ended] + 1, n_units):
                        epilogue_end(ended)
                        ended += 1
                    if begun < len(rows) and ended == begun and u >= begin_at[begun]:
                        epilogue(begun)
                        begun += 1
                        if rows[begun - 1].sweep < 3:
                            ended += 1
            while ended < len(rows):
                if begun == ended:
                    epilogue(begun)
                    begun += 1
                epilogue_end(ended)
                ended += 1

        @block.tensor
        def _(pe):
            pe.wait_ge(s_wready, 1)
            stored = [0]
            xts = [0]

            def need_rows(k):
                if k > stored[0]:
                    pe.wait_ge(s_row, k)
                    stored[0] = k

            def transpose_vector(n):
                row = rows[n]
                if row.sweep == 4:
                    need_rows(row_index[3, row.C] + 1)
                if xts[0]:
                    pe.wait_ge(s_xtc, xts[0])
                src_slot = 0 if row.sweep == 1 else 1
                for c in range(CB):
                    last = nc.tensor.transpose(ps_xt[0:F, P * c:P * c + P], vec[:, CB * row.C + c, src_slot, :], ident[:])
                last.then_inc(s_xt, 1)
                xts[0] += 1

            def epilogue(n):
                row = rows[n]
                pe.wait_ge(s_evac, n + 1)
                need_rows(n)
                if n in x_rows:
                    pe.wait_ge(s_xtc, x_rows.index(n) + 1)
                if row.sweep == 4 and row.C == 0:
                    for ar in range(Q):
                        last = nc.tensor.matmul(ps_deg[32 * ar:32 * ar + 32, :], fold[:],
                                                row_sums[:].rearrange("p c (k a) -> p (c k) a", a=Q)[:, :, ar],
                                                start=True, stop=True)
                    last.then_inc(s_deg, 1)
                for c in range(CB):
                    cols = slice(P * c, P * c + P)
                    S, PR, XT = sum_s[:, cols], sum_p[:, cols], vec_t[:, cols]
                    lin, both = ps_lin[:, c, 0, :], ps_lin[:, c, :, :]
                    if row.sweep == 1:
                        nc.tensor.matmul(both, S, rhs_s1[:], start=True, stop=False)
                        if row.has_pair:
                            nc.tensor.matmul(lin, PR, rhs_p1[:], start=False, stop=False)
                        last = nc.tensor.matmul(lin, XT[0:F, :], rhs_x1[:], start=False, stop=True)
                    elif row.sweep == 2:
                        last = nc.tensor.matmul(both, S, rhs_s2[:], start=True, stop=not row.has_pair)
                        if row.has_pair:
                            last = nc.tensor.matmul(lin, PR, rhs_p2[:], start=False, stop=True)
                    elif row.sweep == 3:
                        if row.has_pair:
                            nc.tensor.matmul(both, PR, rhs_p3[:], start=True, stop=False)
                        last = nc.tensor.matmul(lin, S, rhs_w3[:], start=not row.has_pair, stop=True)
                    else:
                        nc.tensor.matmul(both, XT, rhs_x4[:], start=True, stop=False)
                        last = nc.tensor.matmul(lin, S, ws[:, 1, :], start=False, stop=True)
                if row.sweep in (1, 2) and row.has_pair:
                    for c in range(CB):
                        last = nc.tensor.transpose(ps_tr[:, c, :, :], sum_p[:, P * c:P * c + P], ident[:])
                last.then_inc(s_lin, 1)

            u = 0
            pending = 0
            for n, row in enumerate(rows):
                pair_at = [k for k, (_, kind) in enumerate(row.units) if kind == PAIR]
                single_at = [k for k, (_, kind) in enumerate(row.units) if kind == SINGLE]
                single_slot = {1: 0, 2: 1, 3: 0, 4: 1}[row.sweep]
                if row.sweep == 1 and n == 0:
                    pe.wait_ge(s_x0, 4)
                strip_of_unit = [i for i in range(first_strip[n], first_strip[n + 1]) for _ in strips[i][3]]
                for k, (J, kind) in enumerate(row.units):
                    i = strip_of_unit[k]
                    J0 = strips[i][1]
                    if pending < n and u == epilogue_at[pending]:
                        epilogue(pending)
                        pending += 1
                    if k == min(2, len(row.units) - 1) and n in x_rows:
                        transpose_vector(n)
                    if k == 0 and n >= 2:
                        pe.wait_ge(s_evac, n - 1)
                    need = needed_row(row, J, kind)
                    if need is not None:
                        need_rows(need + 1)
                    pe.wait_ge(s_turned, u + 1)
                    for c in range(CB):
                        chunk = (J - J0) * UC + 32 * c
                        moving = strip_of(i)[:, :, chunk:chunk + 32]
                        if kind == PAIR:
                            last = nc.tensor.matmul(ps_pair[n % 2][:], vec[:, CB * J + c, :, :], moving,
                                                    start=(k == pair_at[0] and c == 0),
                                                    stop=(k == pair_at[-1] and c == CB - 1))
                        else:
                            half = F * (c % 2)
                            last = nc.tensor.matmul(ps_single[n % 2][half:half + F, :],
                                                    vec[:, CB * J + c, single_slot, :], moving,
                                                    start=(k == single_at[0] and c < 2),
                                                    stop=(k == single_at[-1] and c >= CB - 2))
                    last.then_inc(s_unit, 1)
                    u += 1
            while pending < len(rows):
                epilogue(pending)
                pending += 1


_INS = ['x', 'adj', 'L0_gnn_weight', 'L1_gnn_W', 'L1_gnn_b']
_OUTS = [((N, F), 'float32')]


def kernel(**inputs):
    import numpy as _np
    import concourse.bacc as _bacc
    from concourse import mybir as _mybir
    from concourse.bass_utils import run_bass_kernel_spmd as _run

    nc = _bacc.Bacc("TRN2", target_bir_lowering=False, num_devices=1)
    arrays, args = {}, []
    for name in _INS:
        a = _np.ascontiguousarray(inputs[name])
        arrays[f"in_{name}_dram"] = a
        args.append(nc.dram_tensor(f"in_{name}_dram", a.shape, _mybir.dt.from_np(a.dtype), kind="ExternalInput").ap())
    for i, (shape, dtype) in enumerate(_OUTS):
        args.append(nc.dram_tensor(f"out_{i}_dram", shape, _mybir.dt.from_np(_np.dtype(dtype)), kind="ExternalOutput").ap())
    cheb_sage_kernel(nc, *args)
    r = _run(nc, [arrays], core_ids=[0])
    return r.results[0]["out_0_dram"]
```

```python
import concourse.bass as bass
from concourse import mybir
from contextlib import ExitStack

FP32 = mybir.dt.float32
ALU = mybir.AluOpType
ACT = mybir.ActivationFunctionType
AX = mybir.AxisListType

P = 128
N = 8192
F = 64
Q = 4
CH = N // P
CB = 4
NB = CH // CB
BN = CB * P
G = CB * Q
QN = N // Q
W = 4
SW = NB // W
UC = CB * 32
RING = 16
NSEM = 6
LATE_BLOCKS = NB - 4
LATE = 7
NEXT = 1
LEAD = 5
SINGLE, PAIR = 0, 1
LN_EPS = 1e-5
L2_EPS = 1e-12


class Row:

    def __init__(self, sweep, C, strips, final=True):
        self.sweep, self.C, self.strips = sweep, C, strips
        self.final = final
        self.units = [u for _, _, units in strips for u in units]
        self.has_pair = any(kind == PAIR for _, kind in self.units)
        self.has_single = any(kind == SINGLE for _, kind in self.units)
        self.has_late = sweep == 1 and C < LATE_BLOCKS


def sweep_rows():
    rows = []
    for C in range(NB):
        order = [(C // W + 1 + k) % SW for k in range(SW)]
        strips = []
        for s in order:
            Js = list(range(W * s, W * s + W))
            strips.append((Js[0], W, [(J, SINGLE) for J in Js if J >= C] + [(J, PAIR) for J in Js if J < C]))
        rows.append(Row(1, C, strips))
    for C in reversed(range(NB)):
        strips = []
        first = C + 1 if C < LATE_BLOCKS else C
        for s in reversed(range(first // W, SW)):
            Js = list(range(max(first, W * s), W * s + W))
            units = [(J, PAIR if J > C else SINGLE) for J in reversed(Js)]
            if len(units) > 1 and units[-1][0] == C:
                units[-1], units[-2] = units[-2], units[-1]
            strips.append((Js[0], len(Js), units))
        rows.append(Row(2, C, strips))
    for C in range(NB):
        strips = []
        for s in range(C // W + 1):
            Js = list(range(W * s, min(C, W * s + W - 1) + 1))
            units = [(J, PAIR if J < C else SINGLE) for J in Js]
            if len(units) > 1 and units[-1][0] == C:
                units[-1], units[-2] = units[-2], units[-1]
            strips.append((Js[0], len(Js), units))
        rows.append(Row(3, C, strips))

    def upper(C, first, last):
        strips = []
        for s in range(first // W, last // W + 1):
            Js = list(range(max(first, W * s), W * s + W))
            strips.append((Js[0], len(Js), [(J, SINGLE) for J in Js]))
        return strips

    half = NB // 2
    sweep3, rows = rows[-NB:], rows[:-NB]
    for row in sweep3:
        rows.append(row)
        if W <= row.C < 2 * W:
            C = 2 * W - 1 - row.C
            rows.append(Row(4, C, upper(C, C, W - 1), final=False))
        if row.C >= half:
            C = NB - 1 - row.C
            rows.append(Row(4, C, upper(C, max(C, W), (half if C >= W else NB - W) - 1), final=False))
    for C in [0, 8, 4, 9, 1, 5, 10, 15, 6, 2, 11, 14, 12, 3, 7, 13]:
        rows.append(Row(4, C, upper(C, max(C, half if C >= W else NB - W), NB - 1)))
    return rows


def ring_places(strips):
    at, places, live = 0, [], []
    for i, (_, _, w, _) in enumerate(strips):
        if at + w > RING:
            at = 0
        clash = [k for k, lo, hi in live if lo < at + w and hi > at]
        before = max(clash, default=-1) + 1
        before = max(before, i - NSEM + 1)
        live = [(k, lo, hi) for k, lo, hi in live if k >= before] + [(i, at, at + w)]
        places.append((at, before))
        at += w
    return places


def cheb_sage_kernel(nc, x, adj, w_cheb, w_sage, b_sage, out):
    rows = sweep_rows()
    row_index = {(r.sweep, r.C): n for n, r in enumerate(rows) if r.final}
    strips = [(n, J0, w, units) for n, r in enumerate(rows) for J0, w, units in r.strips]
    n_units = sum(len(r.units) for r in rows)
    row_start = [sum(len(r.units) for r in rows[:n]) for n in range(len(rows) + 1)]
    strip_start = [sum(len(s[3]) for s in strips[:i]) for i in range(len(strips) + 1)]
    first_strip = [sum(len(r.strips) for r in rows[:n]) for n in range(len(rows) + 1)]
    places = ring_places(strips)
    x_rows = [n for n, r in enumerate(rows) if r.sweep == 1 or r.sweep == 4 and r.final]

    root_rows = [n for n, r in enumerate(rows) if r.sweep >= 3 and r.final]

    def needed_row(row, J, kind):
        if row.sweep == 1:
            return row_index[1, J] if kind == PAIR else None
        if row.sweep == 2:
            return row_index[2, J] if kind == PAIR else row_index[1, J]
        if row.sweep == 3:
            return row_index[3, J] if kind == PAIR else row_index[2, J]
        return row_index[3, J]

    epilogue_at = []
    for n in range(len(rows)):
        if n + 1 == len(rows):
            epilogue_at.append(n_units)
            continue
        J, kind = rows[n + 1].units[0]
        epilogue_at.append(row_start[n + 1] + (needed_row(rows[n + 1], J, kind) != n))

    first_need = {}
    u = 0
    for row in rows:
        for J, kind in row.units:
            first_need.setdefault(needed_row(row, J, kind), u)
            u += 1
    begin_at = [min(epilogue_at[n] + LEAD, first_need.get(n, n_units) + 1,
                    (epilogue_at + [n_units])[n + 1] + NEXT) for n in range(len(rows))]

    late_at, late_end_at = {}, {}
    for n, r in enumerate(rows):
        if r.has_late:
            late_at[n] = row_start[n + 1] + LATE
            late_end_at[n] = row_start[n + 2] - 1
    late_rows = sorted(late_at)

    adj_v = adj.rearrange("(a c r) m -> a r c m", a=Q, r=32)
    x_v = x.rearrange("(a c q) f -> a q c f", a=Q, q=32)
    out_v = out.rearrange("(a c q) f -> a q c f", a=Q, q=32)

    ctx = ExitStack()
    with ctx:
        def sb(name, shape, dt=FP32):
            return ctx.enter_context(nc.sbuf_tensor(name, shape, dt))

        def sem(name):
            return ctx.enter_context(nc.semaphore(name))

        ring = sb("ring", [P, RING * G * UC])
        vec = sb("vec", [P, CH, 2, F])
        res = sb("res", [P, CH, F])
        part = sb("part", [P, CH, F])
        sum_s = sb("sum_s", [P, BN])
        sum_p = sb("sum_p", [P, BN])
        sum_d = sb("sum_d", [P, BN])
        vec_t = sb("vec_t", [F + 1, BN])
        strip_sums = sb("strip_sums", [P, 2, SW, G])
        row_sums = sb("row_sums", [P, NB, G])
        rdeg = sb("rdeg", [P, CH])
        ident = sb("ident", [P, P])
        fold = sb("fold", [P, 32])
        ws = row_sums[:, 0:2 * F // G, :].rearrange("p c g -> p (c g)").rearrange("p (k f) -> p k f", k=2)
        wb = sb("wb", [P, F])
        rhs_s1 = sb("rhs_s1", [P, 2, F])
        rhs_s2 = sb("rhs_s2", [P, 2, F])
        rhs_w3 = sb("rhs_w3", [P, F])
        rhs_p1 = sb("rhs_p1", [P, F])
        rhs_p2 = sb("rhs_p2", [P, F])
        rhs_p3 = sb("rhs_p3", [P, 2, F])
        rhs_x1 = sb("rhs_x1", [F, F])
        rhs_x4 = sb("rhs_x4", [F + 1, 2, F])
        eps = sb("eps", [P, 1])
        stat = sb("stat", [P, 4, CH])
        tmp = sb("tmp", [P, CB, F])
        wc = tmp

        ps_single = [ctx.enter_context(nc.psum_tensor(f"ps_single{i}", [P, BN], FP32)) for i in range(2)]
        ps_pair = [ctx.enter_context(nc.psum_tensor(f"ps_pair{i}", [P, BN], FP32)) for i in range(2)]
        ps_lin = ctx.enter_context(nc.psum_tensor("ps_lin", [P, CB, 2, F], FP32))
        ps_tr = ctx.enter_context(nc.psum_tensor("ps_tr", [P, CB, 2, F], FP32))
        ps_xt = ctx.enter_context(nc.psum_tensor("ps_xt", [P, BN], FP32))
        ps_late = ctx.enter_context(nc.psum_tensor("ps_late", [P, CB, 2, F], FP32))
        ps_deg = ps_late[:, 0, :, :].rearrange("p a f -> p (a f)")[:, 0:CH]

        def diagonal(C, c):
            if C < NB // 2:
                at = CH // 2 + 8 * c
                return vec[:, at:at + 8, 1, :]
            at = CH - 16 + 8 * (c % 2)
            return vec[:, at:at + 8, 1, :] if c < 2 else part[:, at:at + 8, :]

        def strip_of(i):
            w = strips[i][2]
            at = places[i][0] * G * UC
            return ring[:, at:at + G * w * UC].rearrange("p (g m) -> p g m", g=G)

        s_x = [sem(f"x_loaded{h}") for h in range(2)]
        s_cent = sem("x_centred")
        s_sq = sem("x_squared")
        s_w = sem("weights_loaded")
        s_zero = sem("pool_cleared")
        s_const = sem("constants_ready")
        s_wready = sem("weights_ready")
        s_strip = [sem(f"strip_loaded{i}") for i in range(NSEM)]
        s_turned = sem("units_turned")
        s_unit = sem("units_done")
        s_summed = sem("strips_summed")
        s_late = sem("late_done")
        s_lateev = sem("late_evacuated")
        s_latelin = sem("late_combined")
        s_lateadd = sem("late_added")
        s_evac = sem("rows_evacuated")
        s_xt = sem("xt_made")
        s_xtc = sem("xt_copied")
        s_lin = sem("rows_combined")
        s_read = sem("combinations_read")
        s_row = sem("rows_stored")
        s_x0 = sem("x_normed")
        s_var = sem("variance_ready")
        s_std = sem("std_ready")
        s_degsum = sem("degree_sums_ready")
        s_deg = sem("degrees_folded")
        s_step = sem("dve_steps")
        s_out = sem("out_stored")

        block = ctx.enter_context(nc.Block())

        @block.sync
        def _(sp):
            for h in range(2):
                for a in range(Q):
                    sp.dma_start(res[32 * a:32 * a + 32, 32 * h:32 * h + 32, :], x_v[a, :, 32 * h:32 * h + 32, :])\
                        .then_inc(s_x[h], 16)
            for i, (n, J0, w, _) in enumerate(strips):
                row = rows[n]
                if places[i][1] > 0:
                    sp.wait_ge(s_unit, strip_start[places[i][1]])
                for ar in range(Q):
                    for a in range(Q):
                        col = a * QN + J0 * UC
                        src = adj_v[ar, :, CB * row.C:CB * row.C + CB, col:col + w * UC]
                        dst = strip_of(i)[32 * a:32 * a + 32, ar:G:Q, :]
                        sp.dma_start(dst, src).then_inc(s_strip[i % NSEM], 16)

        @block.gpsimd
        def _(pool):
            nc.gpsimd.memset(ident[:], 0.0).then_inc(s_zero, 1)
            nc.gpsimd.memset(rhs_p3[:], 0.0).then_inc(s_zero, 1)
            nc.gpsimd.memset(rhs_x4[:], 0.0).then_inc(s_zero, 1)
            nc.gpsimd.memset(eps[:], LN_EPS).then_inc(s_zero, 1)
            pool.wait_ge(s_zero, 4)
            nc.gpsimd.affine_select(out=ident[:], in_=ident[:], compare_op=ALU.not_equal, fill=1.0, base=0,
                                    pattern=[[-1, P]], channel_multiplier=1).then_inc(s_const, 1)
            for n, C in sorted((n, C) for (sweep, C), n in row_index.items() if sweep == 4):
                pool.wait_ge(s_row, n + 1)
                for a in range(Q):
                    pool.dma_start(out_v[a, :, CB * C:CB * C + CB, :],
                                   vec[32 * a:32 * a + 32, CB * C:CB * C + CB, 0, :]).then_inc(s_out, 16)
            pool.wait_ge(s_out, 16 * Q * NB)

        @block.scalar
        def _(act):
            wc_v = w_cheb.rearrange("k i o -> i k o")
            ws_v = w_sage.rearrange("(k i) o -> i k o", k=2)
            for half in (0, F):
                act.dma_start(wc[half:half + F, :, :], wc_v).then_inc(s_w, 16)
                act.dma_start(ws[half:half + F, :, :], ws_v).then_inc(s_w, 16)
            act.wait_ge(s_zero, 4)
            act.dma_start(rhs_x4[F:F + 1, 1, :], b_sage.rearrange("(o f) -> o f", o=1)).then_inc(s_w, 16)
            quarter = [slice(16 * k, 16 * k + 16) for k in range(4)]

            def root_of_variance(number, sl):
                act.wait_ge(s_var, number)
                nc.scalar.activation(stat[:, 2, sl], stat[:, 1, sl], ACT.Sqrt, bias=eps[:], scale=1.0 / F)\
                    .then_inc(s_std, 1)

            for k in range(4):
                act.wait_ge(s_cent, k + 1)
                nc.scalar.activation(part[:, quarter[k], :], vec[:, quarter[k], 0, :], ACT.Square).then_inc(s_sq, 1)
                if k:
                    root_of_variance(k, quarter[k - 1])
            root_of_variance(4, quarter[3])
            roots = 4

            def sum_rows(i):
                n, J0, w, _ = strips[i]
                C = rows[n].C
                if rows[n].sweep > 1:
                    return
                act.wait_ge(s_strip[i % NSEM], 16 * Q * Q * (i // NSEM + 1))
                if C >= 2:
                    act.wait_ge(s_degsum, C - 1)
                for g in range(G):
                    last = nc.scalar.activation(strip_of(i)[:, g, :], strip_of(i)[:, g, :], ACT.Copy,
                                                accum_out=strip_sums[:, C % 2, J0 // W, g:g + 1])
                last.then_inc(s_summed, 1)

            sum_rows(0)
            for n, row in enumerate(rows):
                first = first_strip[n]
                if first + 1 < first_strip[n + 1]:
                    sum_rows(first + 1)
                if n in x_rows:
                    act.wait_ge(s_xt, x_rows.index(n) + 1)
                    if x_rows.index(n):
                        act.wait_ge(s_lin, x_rows[x_rows.index(n) - 1] + 1)
                    nc.scalar.activation(vec_t[0:F, :], ps_xt[0:F, :], ACT.Copy).then_inc(s_xtc, 1)
                for i in range(first + 2, first_strip[n + 1]):
                    sum_rows(i)
                if n - 1 in late_at:
                    act.wait_ge(s_late, late_rows.index(n - 1) + 1)
                    if late_rows.index(n - 1):
                        act.wait_ge(s_latelin, late_rows.index(n - 1))
                    nc.scalar.activation(sum_d[:], ps_single[(n - 1) % 2][:], ACT.Copy).then_inc(s_lateev, 1)
                if n + 1 < len(rows):
                    sum_rows(first_strip[n + 1])
                act.wait_ge(s_unit, row_start[n + 1])
                if n:
                    act.wait_ge(s_lin, n)
                if row.has_single:
                    last = nc.scalar.activation(sum_s[:], ps_single[n % 2][:], ACT.Copy)
                if row.has_pair:
                    last = nc.scalar.activation(sum_p[:], ps_pair[n % 2][:], ACT.Copy)
                last.then_inc(s_evac, 1)
                if n in root_rows:
                    roots += 1
                    sl = slice(CB * row.C, CB * row.C + CB)
                    if row.sweep == 3:
                        root_of_variance(roots, sl)
                    else:
                        act.wait_ge(s_var, roots)
                        nc.scalar.activation(stat[:, 2, sl], stat[:, 1, sl], ACT.Sqrt).then_inc(s_std, 1)

        @block.vector
        def _(dve):
            steps = [0]

            def then(ins):
                steps[0] += 1
                ins.then_inc(s_step, 1)
                dve.wait_ge(s_step, steps[0])

            def per_node(ap, k):
                return ap.unsqueeze(2).broadcast_to([P, k, F])

            def centre(dst, src, sl, k):
                then(nc.vector.reduce_sum(stat[:, 0, sl], src, AX.X))
                then(nc.vector.tensor_scalar(stat[:, 0, sl], stat[:, 0, sl], -1.0 / F, None, ALU.mult))
                return nc.vector.tensor_tensor(dst, src, per_node(stat[:, 0, sl], k), ALU.add)

            def scale_relu(dst, sl, k, root):
                dve.wait_ge(s_std, root)
                then(nc.vector.reciprocal(stat[:, 3, sl], stat[:, 2, sl]))
                return nc.vector.scalar_tensor_tensor(out=dst, in0=dst, scalar=0.0, in1=per_node(stat[:, 3, sl], k),
                                                      op0=ALU.max, op1=ALU.mult)

            quarter = [slice(16 * k, 16 * k + 16) for k in range(4)]
            for k in range(6):
                if k < 4:
                    dve.wait_ge(s_x[k // 2], 16 * Q)
                    centre(vec[:, quarter[k], 0, :], res[:, quarter[k], :], quarter[k], 16).then_inc(s_cent, 1)
                if 1 <= k < 5:
                    dve.wait_ge(s_sq, k)
                    nc.vector.reduce_sum(stat[:, 1, quarter[k - 1]], part[:, quarter[k - 1], :], AX.X).then_inc(s_var, 1)
                if k >= 2:
                    scale_relu(vec[:, quarter[k - 2], 0, :], quarter[k - 2], 16, k - 1).then_inc(s_x0, 1)
            dve.wait_ge(s_w, 16 * 5)
            dve.wait_ge(s_const, 1)
            lo, hi = slice(0, F), slice(F, P)
            nc.vector.memset(vec_t[F:F + 1, :], 1.0)
            nc.vector.tensor_tensor(rhs_s1[:, 0, :], wc[:, 1, :], wc[:, 3, :], ALU.subtract)
            nc.vector.tensor_scalar(rhs_s2[:, 0, :], wc[:, 2, :], 2.0, None, ALU.mult)
            nc.vector.tensor_scalar(rhs_w3[:], wc[:, 3, :], 2.0, None, ALU.mult)
            for dst in (rhs_s1, rhs_s2):
                nc.vector.tensor_tensor(dst[:, 1, :], ident[:, lo], ident[:, hi], ALU.add)
            nc.vector.tensor_tensor(rhs_p1[lo, :], wc[lo, 1, :], wc[lo, 3, :], ALU.subtract)
            nc.vector.tensor_scalar(rhs_p1[hi, :], wc[hi, 2, :], 2.0, None, ALU.mult)
            nc.vector.tensor_scalar(rhs_p2[lo, :], wc[lo, 3, :], 2.0, None, ALU.mult)
            nc.vector.tensor_scalar(rhs_p2[hi, :], wc[hi, 2, :], 2.0, None, ALU.mult)
            nc.vector.tensor_scalar(rhs_p3[lo, 0, :], wc[lo, 3, :], 2.0, None, ALU.mult)
            nc.vector.tensor_copy(rhs_p3[hi, 1, :], ws[hi, 1, :])
            nc.vector.tensor_copy(wb[:], ws[:, 1, :])
            nc.vector.tensor_tensor(rhs_x1[:], wc[lo, 0, :], wc[lo, 2, :], ALU.subtract)
            nc.vector.tensor_copy(rhs_x4[lo, 0, :], ws[lo, 1, :])
            nc.vector.tensor_copy(rhs_x4[lo, 1, :], ws[lo, 0, :])
            for a in range(Q):
                last = nc.vector.tensor_copy(fold[32 * a:32 * a + 32, :], ident[32 * a:32 * a + 32, 32 * a:32 * a + 32])
            last.then_inc(s_wready, 1)

            roots = [4]

            def epilogue(n):
                row = rows[n]
                C = row.C
                sl = slice(CB * C, CB * C + CB)
                x1, pt = res[:, sl, :], part[:, sl, :]
                lin, new, tr = ps_lin[:, :, 0, :], ps_lin[:, :, 1, :], ps_tr
                if row.sweep == 4 and row.final and C == 0:
                    dve.wait_ge(s_deg, 1)
                    then(nc.vector.tensor_scalar(rdeg[:], ps_deg[:], 1.0, 1.0, ALU.add, ALU.max))
                    then(nc.vector.reciprocal(rdeg[:], rdeg[:]))
                dve.wait_ge(s_lin, n + 1)
                if n:
                    dve.wait_ge(s_row, n)
                if row.sweep == 1:
                    dve.wait_ge(s_summed, SW * (C + 1))
                    nc.vector.reduce_sum(row_sums[:, C, :], strip_sums[:, C % 2].rearrange("p s g -> p g s"), AX.X)\
                        .then_inc(s_degsum, 1)
                    nc.vector.tensor_tensor(x1, x1, lin, ALU.add)
                    if row.has_pair:
                        nc.vector.tensor_copy(pt, tr[:, :, 1, :])
                        then(nc.vector.tensor_copy(vec[:, sl, 1, :], new))
                        last = nc.vector.tensor_tensor(vec[:, sl, 1, :], vec[:, sl, 1, :], tr[:, :, 0, :], ALU.add)
                    else:
                        nc.vector.memset(pt, 0.0)
                        last = nc.vector.tensor_copy(vec[:, sl, 1, :], new)
                elif row.sweep == 2:
                    then(nc.vector.tensor_tensor(x1, x1, lin, ALU.add))
                    if row.has_single:
                        then(nc.vector.tensor_tensor(tmp[:], pt, new, ALU.add))
                    if row.has_pair:
                        then(nc.vector.tensor_tensor(tmp[:], tmp[:] if row.has_single else pt, tr[:, :, 1, :], ALU.add))
                    last = nc.vector.scalar_tensor_tensor(out=vec[:, sl, 0, :], in0=tmp[:], scalar=2.0,
                                                          in1=vec[:, sl, 0, :], op0=ALU.mult, op1=ALU.subtract)
                elif row.sweep == 3:
                    then(nc.vector.tensor_tensor(x1, x1, lin, ALU.add))
                    if row.has_pair:
                        last = nc.vector.tensor_copy(pt, new)
                    else:
                        last = nc.vector.memset(pt, 0.0)
                    last.then_inc(s_read, 1)
                    then(centre(vec[:, sl, 1, :], x1, sl, CB))
                    then(nc.vector.tensor_tensor(tmp[:], vec[:, sl, 1, :], vec[:, sl, 1, :], ALU.mult))
                    nc.vector.reduce_sum(stat[:, 1, sl], tmp[:], AX.X).then_inc(s_var, 1)
                    return
                elif not row.final:
                    last = nc.vector.tensor_tensor(pt, pt, lin, ALU.add)
                else:
                    then(nc.vector.tensor_tensor(tmp[:], pt, lin, ALU.add))
                    then(nc.vector.tensor_tensor(tmp[:], tmp[:], per_node(rdeg[:, sl], CB), ALU.mult))
                    nc.vector.tensor_tensor(tmp[:], tmp[:], new, ALU.add).then_inc(s_read, 1)
                    dve.wait_ge(s_read, root_rows.index(n) + 1)
                    then(nc.vector.tensor_scalar(tmp[:], tmp[:], 0.0, None, ALU.max))
                    then(nc.vector.tensor_tensor(vec[:, sl, 0, :], tmp[:], tmp[:], ALU.mult))
                    nc.vector.reduce_sum(stat[:, 1, sl], vec[:, sl, 0, :], AX.X).then_inc(s_var, 1)
                    return
                last.then_inc(s_row, 1)

            def epilogue_end(n):
                row = rows[n]
                sl = slice(CB * row.C, CB * row.C + CB)
                roots[0] += 1
                if row.sweep == 3:
                    last = scale_relu(vec[:, sl, 1, :], sl, CB, roots[0])
                else:
                    dve.wait_ge(s_std, roots[0])
                    then(nc.vector.tensor_scalar(stat[:, 3, sl], stat[:, 2, sl], L2_EPS, None, ALU.max))
                    then(nc.vector.reciprocal(stat[:, 3, sl], stat[:, 3, sl]))
                    then(nc.vector.tensor_tensor(tmp[:], tmp[:], per_node(stat[:, 3, sl], CB), ALU.mult))
                    last = nc.vector.tensor_tensor(vec[:, sl, 0, :], tmp[:], res[:, sl, :], ALU.add)
                last.then_inc(s_row, 1)

            def late_epilogue(n):
                sl = slice(CB * rows[n].C, CB * rows[n].C + CB)
                dve.wait_ge(s_latelin, late_rows.index(n) + 1)
                nc.vector.tensor_tensor(res[:, sl, :], res[:, sl, :], ps_late[:, :, 0, :], ALU.add)
                nc.vector.tensor_tensor(part[:, sl, :], part[:, sl, :], ps_late[:, :, 1, :], ALU.add)\
                    .then_inc(s_lateadd, 1)

            late = 0
            begun = ended = 0
            u = 0
            for i, (n, J0, w, units) in enumerate(strips):
                dve.wait_ge(s_strip[i % NSEM], 16 * Q * Q * (i // NSEM + 1))
                if rows[n].sweep == 1:
                    dve.wait_ge(s_summed, i + 1)
                for J, _ in units:
                    col = (J - J0) * UC
                    if rows[n].has_late and J == rows[n].C:
                        if J > 0:
                            dve.wait_ge(s_late, J)
                        for c in range(CB):
                            src = strip_of(i)[:, :, col + 32 * c:col + 32 * c + 32].rearrange("p (k h) q -> p k h q", h=2)
                            dst = diagonal(J, c).rearrange("p k (h r) -> p k h r", h=2)
                            last = nc.vector.transpose(dst, src)
                        last.then_inc(s_turned, 1)
                    else:
                        blocks = strip_of(i)[:, :, col:col + UC].rearrange("p g (c q) -> p g c q", q=32)
                        nc.vector.transpose(blocks, blocks).then_inc(s_turned, 1)
                    u += 1
                    if ended < begun and u >= min(begin_at[ended] + 1, n_units):
                        epilogue_end(ended)
                        ended += 1
                    if begun < len(rows) and ended == begun and u >= begin_at[begun]:
                        epilogue(begun)
                        begun += 1
                        if begun - 1 not in root_rows:
                            ended += 1
                    if late < len(late_rows) and ended > late_rows[late] and u >= min(late_end_at[late_rows[late]] + LEAD,
                                                                                      row_start[late_rows[late] + 2]):
                        late_epilogue(late_rows[late])
                        late += 1
            while ended < len(rows):
                if begun == ended:
                    epilogue(begun)
                    begun += 1
                epilogue_end(ended)
                ended += 1

        @block.tensor
        def _(pe):
            pe.wait_ge(s_wready, 1)
            stored = [0]
            xts = [0]

            def need_rows(k):
                if k > stored[0]:
                    pe.wait_ge(s_row, k)
                    stored[0] = k

            def transpose_vector(n):
                row = rows[n]
                if row.sweep == 4:
                    need_rows(row_index[3, row.C] + 1)
                if xts[0]:
                    pe.wait_ge(s_xtc, xts[0])
                src_slot = 0 if row.sweep == 1 else 1
                for c in range(CB):
                    last = nc.tensor.transpose(ps_xt[0:F, P * c:P * c + P], vec[:, CB * row.C + c, src_slot, :], ident[:])
                last.then_inc(s_xt, 1)
                xts[0] += 1

            def late_product(n):
                C = rows[n].C
                need_rows(n + 1)
                for c in range(CB):
                    half = F * (c % 2)
                    last = nc.tensor.matmul(ps_single[n % 2][half:half + F, :], vec[:, CB * C + c, 1, :],
                                            diagonal(C, c), start=(c < 2), stop=(c >= CB - 2))
                last.then_inc(s_late, 1)

            def late_epilogue(n):
                late = late_rows.index(n)
                pe.wait_ge(s_lateev, late + 1)
                if late:
                    pe.wait_ge(s_lateadd, late)
                for c in range(CB):
                    D = sum_d[:, P * c:P * c + P]
                    last = nc.tensor.matmul(ps_late[:, c, :, :], D, rhs_s2[:], start=True, stop=True)
                last.then_inc(s_latelin, 1)

            def epilogue(n):
                row = rows[n]
                pe.wait_ge(s_evac, n + 1)
                if n - 1 in root_rows:
                    pe.wait_ge(s_read, root_rows.index(n - 1) + 1)
                else:
                    need_rows(n)
                if n in x_rows:
                    pe.wait_ge(s_xtc, x_rows.index(n) + 1)
                if row.sweep == 4 and row.final and row.C == 0:
                    pe.wait_ge(s_lateadd, len(late_rows))
                    for ar in range(Q):
                        last = nc.tensor.matmul(ps_deg[32 * ar:32 * ar + 32, :], fold[:],
                                                row_sums[:].rearrange("p c (k a) -> p (c k) a", a=Q)[:, :, ar],
                                                start=True, stop=True)
                    last.then_inc(s_deg, 1)
                for c in range(CB):
                    cols = slice(P * c, P * c + P)
                    S, PR, XT = sum_s[:, cols], sum_p[:, cols], vec_t[:, cols]
                    lin, both = ps_lin[:, c, 0, :], ps_lin[:, c, :, :]
                    if row.sweep == 1:
                        nc.tensor.matmul(both, S, rhs_s1[:], start=True, stop=False)
                        if row.has_pair:
                            nc.tensor.matmul(lin, PR, rhs_p1[:], start=False, stop=False)
                        last = nc.tensor.matmul(lin, XT[0:F, :], rhs_x1[:], start=False, stop=True)
                    elif row.sweep == 2:
                        if row.has_single:
                            last = nc.tensor.matmul(both, S, rhs_s2[:], start=True, stop=not row.has_pair)
                        if row.has_pair:
                            last = nc.tensor.matmul(lin, PR, rhs_p2[:], start=not row.has_single, stop=True)
                    elif row.sweep == 3:
                        if row.has_pair:
                            nc.tensor.matmul(both, PR, rhs_p3[:], start=True, stop=False)
                        last = nc.tensor.matmul(lin, S, rhs_w3[:], start=not row.has_pair, stop=True)
                    else:
                        if row.final:
                            nc.tensor.matmul(both, XT, rhs_x4[:], start=True, stop=False)
                        last = nc.tensor.matmul(lin, S, wb[:], start=not row.final, stop=True)
                if row.sweep in (1, 2) and row.has_pair:
                    for c in range(CB):
                        last = nc.tensor.transpose(ps_tr[:, c, :, :], sum_p[:, P * c:P * c + P], ident[:])
                last.then_inc(s_lin, 1)

            u = 0
            pending = 0
            for n, row in enumerate(rows):
                pair_at = [k for k, (_, kind) in enumerate(row.units) if kind == PAIR]
                single_at = [k for k, (_, kind) in enumerate(row.units) if kind == SINGLE]
                single_slot = {1: 0, 2: 1, 3: 0, 4: 1}[row.sweep]
                if row.sweep == 1 and n == 0:
                    pe.wait_ge(s_x0, 4)
                strip_of_unit = [i for i in range(first_strip[n], first_strip[n + 1]) for _ in strips[i][3]]
                for k, (J, kind) in enumerate(row.units):
                    i = strip_of_unit[k]
                    J0 = strips[i][1]
                    if pending < n and u == epilogue_at[pending]:
                        epilogue(pending)
                        pending += 1
                    if n - 1 in late_at and u == late_at[n - 1]:
                        late_product(n - 1)
                    if n - 1 in late_at and u == late_end_at[n - 1]:
                        late_epilogue(n - 1)
                    if k == min(2, len(row.units) - 1) and n in x_rows:
                        transpose_vector(n)
                    if k == 0 and n >= 2:
                        pe.wait_ge(s_evac, n - 1)
                    need = needed_row(row, J, kind)
                    if need is not None:
                        need_rows(need + 1)
                    pe.wait_ge(s_turned, u + 1)
                    for c in range(CB):
                        chunk = (J - J0) * UC + 32 * c
                        moving = strip_of(i)[:, :, chunk:chunk + 32]
                        if row.has_late and J == row.C:
                            moving = diagonal(J, c)
                        if kind == PAIR:
                            last = nc.tensor.matmul(ps_pair[n % 2][:], vec[:, CB * J + c, :, :], moving,
                                                    start=(k == pair_at[0] and c == 0),
                                                    stop=(k == pair_at[-1] and c == CB - 1))
                        else:
                            half = F * (c % 2)
                            last = nc.tensor.matmul(ps_single[n % 2][half:half + F, :],
                                                    vec[:, CB * J + c, single_slot, :], moving,
                                                    start=(k == single_at[0] and c < 2),
                                                    stop=(k == single_at[-1] and c >= CB - 2))
                    last.then_inc(s_unit, 1)
                    u += 1
            while pending < len(rows):
                epilogue(pending)
                pending += 1


_INS = ['x', 'adj', 'L0_gnn_weight', 'L1_gnn_W', 'L1_gnn_b']
_OUTS = [((N, F), 'float32')]


def kernel(**inputs):
    import numpy as _np
    import concourse.bacc as _bacc
    from concourse import mybir as _mybir
    from concourse.bass_utils import run_bass_kernel_spmd as _run

    nc = _bacc.Bacc("TRN2", target_bir_lowering=False, num_devices=1)
    arrays, args = {}, []
    for name in _INS:
        a = _np.ascontiguousarray(inputs[name])
        arrays[f"in_{name}_dram"] = a
        args.append(nc.dram_tensor(f"in_{name}_dram", a.shape, _mybir.dt.from_np(a.dtype), kind="ExternalInput").ap())
    for i, (shape, dtype) in enumerate(_OUTS):
        args.append(nc.dram_tensor(f"out_{i}_dram", shape, _mybir.dt.from_np(_np.dtype(dtype)), kind="ExternalOutput").ap())
    cheb_sage_kernel(nc, *args)
    r = _run(nc, [arrays], core_ids=[0])
    return r.results[0]["out_0_dram"]
```
